# Optimizing a Trainium2 kernel written in Bass

```python
import numpy as np
import jax
import jax.numpy as jnp

def _softmax(x, axis=-1):
    return jax.nn.softmax(x, axis=axis)

def _gelu(x):
    return jax.nn.gelu(x, approximate=True)

def _silu(x):
    return jax.nn.silu(x)

def _sigmoid(x):
    return jax.nn.sigmoid(x)

def _layernorm(x, axis=-1, eps=1e-05):
    m = jnp.mean(x, axis=axis, keepdims=True)
    v = jnp.var(x, axis=axis, keepdims=True)
    return (x - m) / jnp.sqrt(v + eps)

def _scatter_add(tgt, idx, src, axis=0):
    return tgt.at[idx].add(src)

def _segment_sum(src, seg, n):
    return jax.ops.segment_sum(src, seg, n)
kernel_name = 'mk_dlrm_tower_d1_rec_r8_a2825f'

def setup_inputs(seed: int=0):
    np.random.seed(seed)
    _w = jnp.asarray

    def _rec_inputs():
        import jax
        import jax.numpy as jnp
        _tk = jax.random.key(seed)
        dense_ctx = jax.random.normal(jax.random.fold_in(_tk, 190), (512, 16), jnp.float32)
        ids = jnp.stack([jax.random.randint(jax.random.fold_in(_tk, 200 + f), (512,), 0, v, jnp.int32) for f, v in enumerate([1250, 1250, 1250, 1250, 1000, 12500, 1250, 1000])], axis=1)
        tbl_0 = 0.05 * jax.random.normal(jax.random.fold_in(_tk, 500 + 0), (1250, 1024), jnp.float32)
        tbl_1 = 0.05 * jax.random.normal(jax.random.fold_in(_tk, 500 + 1), (1250, 1024), jnp.float32)
        tbl_2 = 0.05 * jax.random.normal(jax.random.fold_in(_tk, 500 + 2), (1250, 1024), jnp.float32)
        tbl_3 = 0.05 * jax.random.normal(jax.random.fold_in(_tk, 500 + 3), (1250, 1024), jnp.float32)
        tbl_4 = 0.05 * jax.random.normal(jax.random.fold_in(_tk, 500 + 4), (1000, 1024), jnp.float32)
        tbl_5 = 0.05 * jax.random.normal(jax.random.fold_in(_tk, 500 + 5), (12500, 1024), jnp.float32)
        tbl_6 = 0.05 * jax.random.normal(jax.random.fold_in(_tk, 500 + 6), (1250, 1024), jnp.float32)
        tbl_7 = 0.05 * jax.random.normal(jax.random.fold_in(_tk, 500 + 7), (1000, 1024), jnp.float32)
        _rk = jax.random.fold_in(_tk, 7)
        W_top1 = 0.0310087 * jax.random.normal(jax.random.fold_in(_tk, 801), (1040, 512), jnp.float32)
        W_top2 = 0.0441942 * jax.random.normal(jax.random.fold_in(_tk, 802), (512, 256), jnp.float32)
        W_top3 = 0.0625 * jax.random.normal(jax.random.fold_in(_tk, 803), (256, 1), jnp.float32)
        b_top1 = jnp.zeros((512,), jnp.float32)
        b_top2 = jnp.zeros((256,), jnp.float32)
        return (dense_ctx, ids, tbl_0, tbl_1, tbl_2, tbl_3, tbl_4, tbl_5, tbl_6, tbl_7, W_top1, b_top1, W_top2, b_top2, W_top3)
    dense_ctx, ids, tbl_0, tbl_1, tbl_2, tbl_3, tbl_4, tbl_5, tbl_6, tbl_7, W_top1, b_top1, W_top2, b_top2, W_top3 = _rec_inputs()

    def _L0_rec_setup():
        import jax, jax.numpy as jnp
        import numpy as np
        B, F, H = (1024, 8, 1024)

        def _linear_params(key, fan_in, fan_out):
            kw, kb = jax.random.split(key)
            w = jax.random.normal(kw, (fan_in, fan_out), dtype=jnp.float32) * 0.02
            b = jax.random.normal(kb, (fan_out,), dtype=jnp.float32) * 0.02
            return (w, b)
        key = jax.random.key(seed)
        ks = jax.random.split(key, 7)
        field_vectors = jax.random.normal(ks[0], (B, F, H), dtype=jnp.float32)
        Wn1, bn1 = _linear_params(ks[1], H, H)
        Wn2, bn2 = _linear_params(ks[2], H, H)
        Wa1, ba1 = _linear_params(ks[3], 2 * H, H)
        Wa2, ba2 = _linear_params(ks[4], H, H)
        Wo1, bo1 = _linear_params(ks[5], 2 * H, H)
        Wo2, bo2 = _linear_params(ks[6], H, H)
        not_idx = jnp.array([2, 3], dtype=jnp.int64)
        and_pairs = jnp.array([[0, 1], [2, 3]], dtype=jnp.int64)
        or_pairs = jnp.array([[4, 5]], dtype=jnp.int64)
        return {'field_vectors': field_vectors, 'Wn1': Wn1, 'bn1': bn1, 'Wn2': Wn2, 'bn2': bn2, 'Wa1': Wa1, 'ba1': ba1, 'Wa2': Wa2, 'ba2': ba2, 'Wo1': Wo1, 'bo1': bo1, 'Wo2': Wo2, 'bo2': bo2, 'not_idx': not_idx, 'and_pairs': and_pairs, 'or_pairs': or_pairs}
    _L0_rec_all = _L0_rec_setup()
    _L0_rec_in = {k: v for k, v in _L0_rec_all.items() if k in ('Wn1', 'bn1', 'Wn2', 'bn2', 'Wa1', 'ba1', 'Wa2', 'ba2', 'Wo1', 'bo1', 'Wo2', 'bo2', 'not_idx', 'and_pairs', 'or_pairs')}
    del _L0_rec_all
    return {'dense_ctx': dense_ctx, 'ids': ids, 'tbl_0': tbl_0, 'tbl_1': tbl_1, 'tbl_2': tbl_2, 'tbl_3': tbl_3, 'tbl_4': tbl_4, 'tbl_5': tbl_5, 'tbl_6': tbl_6, 'tbl_7': tbl_7, 'W_top1': W_top1, 'b_top1': b_top1, 'W_top2': W_top2, 'b_top2': b_top2, 'W_top3': W_top3, 'L0_rec_Wn1': _L0_rec_in['Wn1'], 'L0_rec_bn1': _L0_rec_in['bn1'], 'L0_rec_Wn2': _L0_rec_in['Wn2'], 'L0_rec_bn2': _L0_rec_in['bn2'], 'L0_rec_Wa1': _L0_rec_in['Wa1'], 'L0_rec_ba1': _L0_rec_in['ba1'], 'L0_rec_Wa2': _L0_rec_in['Wa2'], 'L0_rec_ba2': _L0_rec_in['ba2'], 'L0_rec_Wo1': _L0_rec_in['Wo1'], 'L0_rec_bo1': _L0_rec_in['bo1'], 'L0_rec_Wo2': _L0_rec_in['Wo2'], 'L0_rec_bo2': _L0_rec_in['bo2'], 'L0_rec_not_idx': _L0_rec_in['not_idx'], 'L0_rec_and_pairs': _L0_rec_in['and_pairs'], 'L0_rec_or_pairs': _L0_rec_in['or_pairs']}

def reference(dense_ctx, ids, tbl_0, tbl_1, tbl_2, tbl_3, tbl_4, tbl_5, tbl_6, tbl_7, W_top1, b_top1, W_top2, b_top2, W_top3, L0_rec_Wn1, L0_rec_bn1, L0_rec_Wn2, L0_rec_bn2, L0_rec_Wa1, L0_rec_ba1, L0_rec_Wa2, L0_rec_ba2, L0_rec_Wo1, L0_rec_bo1, L0_rec_Wo2, L0_rec_bo2, L0_rec_not_idx, L0_rec_and_pairs, L0_rec_or_pairs):
    import jax
    import jax.numpy as jnp

    def _L0_rec_ref(field_vectors, Wn1, bn1, Wn2, bn2, Wa1, ba1, Wa2, ba2, Wo1, bo1, Wo2, bo2, not_idx, and_pairs, or_pairs):
        import jax, jax.numpy as jnp
        import numpy as np
        B, F, H = (1024, 8, 1024)

        def _linear_params(key, fan_in, fan_out):
            kw, kb = jax.random.split(key)
            w = jax.random.normal(kw, (fan_in, fan_out), dtype=jnp.float32) * 0.02
            b = jax.random.normal(kb, (fan_out,), dtype=jnp.float32) * 0.02
            return (w, b)
        num_fields = field_vectors.shape[1]
        x_not = jnp.take(field_vectors, not_idx, axis=1)
        t = jnp.tanh(jax.nn.relu(x_not @ Wn1 + bn1) @ Wn2 + bn2)
        iv = field_vectors.at[:, not_idx, :].set(t)

        def pair_fuse(pairs, W1, b1, W2, b2):
            v = jnp.concatenate([jnp.take(iv, pairs[:, 0], axis=1), jnp.take(iv, pairs[:, 1], axis=1)], axis=-1)
            return jax.nn.relu(v @ W1 + b1) @ W2 + b2
        and_out = pair_fuse(and_pairs, Wa1, ba1, Wa2, ba2)
        or_out = pair_fuse(or_pairs, Wo1, bo1, Wo2, bo2)
        processed = jnp.zeros((num_fields,), dtype=field_vectors.dtype).at[and_pairs.reshape(-1)].set(1.0).at[or_pairs.reshape(-1)].set(1.0)
        remaining = 1.0 - processed
        sum_res = and_out.sum(axis=1) + or_out.sum(axis=1) + jnp.einsum('bfh,f->bh', iv, remaining)
        count = and_pairs.shape[0] + or_pairs.shape[0] + remaining.sum()
        return sum_res / count
    e = jnp.stack([tbl_0[ids[:, 0]], tbl_1[ids[:, 1]], tbl_2[ids[:, 2]], tbl_3[ids[:, 3]], tbl_4[ids[:, 4]], tbl_5[ids[:, 5]], tbl_6[ids[:, 6]], tbl_7[ids[:, 7]]], axis=1)
    z = _L0_rec_ref(e, L0_rec_Wn1, L0_rec_bn1, L0_rec_Wn2, L0_rec_bn2, L0_rec_Wa1, L0_rec_ba1, L0_rec_Wa2, L0_rec_ba2, L0_rec_Wo1, L0_rec_bo1, L0_rec_Wo2, L0_rec_bo2, L0_rec_not_idx, L0_rec_and_pairs, L0_rec_or_pairs)
    z = z.reshape(z.shape[0], -1)
    h = jnp.concatenate([z, dense_ctx], axis=1)
    h = jnp.maximum(h @ W_top1 + b_top1, 0.0)
    h = jnp.maximum(h @ W_top2 + b_top2, 0.0)
    y = h @ W_top3
    return y

_drawn_inputs = setup_inputs


def setup_inputs(seed=0):
    import zlib

    import numpy as np

    out = dict(_drawn_inputs(seed))
    spreads = {'b_top1': (0.0, 0.1), 'b_top2': (0.0, 0.1)}
    factors = {'tbl_0': 4.332,
     'tbl_1': 4.528,
     'tbl_2': 8.0,
     'tbl_3': 8.0,
     'tbl_4': 4.766,
     'tbl_5': 4.729,
     'L0_rec_Wn1': 8.0,
     'L0_rec_bn1': 8.0,
     'L0_rec_Wn2': 8.0,
     'L0_rec_bn2': 8.0,
     'L0_rec_Wa1': 2.948,
     'L0_rec_ba1': 3.815,
     'L0_rec_Wo1': 3.554,
     'L0_rec_bo1': 7.943,
     'L0_rec_Wo2': 2.855}
    for name, (base, spread) in spreads.items():
        noise = np.random.default_rng([zlib.crc32(name.encode()), seed]).standard_normal(out[name].shape)
        drawn = base * np.exp(spread * noise) if base else spread * noise
        out[name] = jnp.asarray(drawn.astype(out[name].dtype))
    for name, factor in factors.items():
        out[name] = (out[name] * factor).astype(out[name].dtype)
    return out
```

```python
from contextlib import ExitStack

import concourse.bass as bass
from concourse import mybir

FP32 = mybir.dt.float32
FP32R = mybir.dt.float32r
INT32 = mybir.dt.int32
ALU = mybir.AluOpType
ACT = mybir.ActivationFunctionType
AX = mybir.AxisListType

P = 128
B = 512
F = 8
H = 1024
KT = H // P
Q = 4
QC = H // Q
GROUPS = B // 32
BT = B // P
D1, D2, DENSE = 512, 256, 16

SLOTS = 8
PAIR_SLOTS = SLOTS - 2
STAGE = 4

BUFS = 5
SLOT_BUF = [0, 3, 4, 3, 2, 4, 2, 4]
H_BUF, T0_BUF, T1_BUF, AND_BUF, OR_BUF, Z_BUF, TOP_BUF = 1, 0, 1, 3, 2, 4, 0

UNIT_WEIGHTS = [0, 0, 1, 1, 2, 3, 2, 3, 4, 5, 6, 7]
UNITS = len(UNIT_WEIGHTS)
UNIT_FILLS = [1, 2, 3, None, 4, 5, None, 6, 7, None, None, None]
FILL_NEEDS = [0, 0, 0, 2, 4, 5, 7, 8]
TOP1_PIECES = D1 // P
PIECES = UNITS * KT + TOP1_PIECES + 1
WEIGHT_BLOCKS = 8 * KT + TOP1_PIECES + 1

NOT_EV, AND0_EV, AND1_EV, OR_EV, FINAL_EV = 4 * KT, 5 * KT, 6 * KT, 7 * KT, 8 * KT

BN1, BN2, BA1, BO1, BA2, BO2, BT1, BT2, W3 = 0, 8, 16, 24, 32, 40, 48, 52, 54
COLS = 56
C_ROW4, C_ROW, C_FIELD, C_BUF, C_IDENT = 0, 8, 16, 24, 32
CONSTS = C_IDENT + P


def dlrm_tower(nc, table, ids_by_group, ids_by_tile, picks, weights, cols, consts, dense_t, w_dense, out, zero_row):
    table_quarters = table.rearrange("v (q c) -> (v q) c", q=Q)

    with ExitStack() as ctx:
        def sb(name, shape, dt):
            return ctx.enter_context(nc.sbuf_tensor(name, shape, dt))

        def sem(name):
            return ctx.enter_context(nc.semaphore(name))

        X = sb("X", [P, BUFS, 2, KT, B], FP32R)
        V = sb("V", [P, KT, B], FP32)
        w_raw = sb("w_raw", [P, 2, KT * P], FP32)
        W = sb("W", [P, 2, 2, KT, P], FP32R)
        gathered = sb("gathered", [P, STAGE, QC], FP32)
        turned = sb("turned", [P, 2, KT, 32], FP32)
        ident = sb("ident", [P, P], FP32R)
        col = sb("col", [P, COLS], FP32)
        rows = sb("rows", [P, SLOTS, GROUPS], INT32)
        rows_rest = sb("rows_rest", [P, BT, F], INT32)
        tab = sb("tab", [P, 8], INT32)
        inv = sb("inv", [P, 1], FP32)
        final_bias = sb("final_bias", [P, KT], FP32)
        PS = ctx.enter_context(nc.psum_tensor("PS", [P, KT, B], FP32))

        Vf = V[:, :, :].rearrange("p k b -> p (k b)")
        turned_f = turned[:, :, :, :].rearrange("p e k b -> p e (k b)")
        W_f = W[:, :, :, :, :].rearrange("p r s k m -> p r s (k m)")
        at = [0]

        def scratch(n):
            at[0] += n
            return Vf[:, at[0] - n:at[0]]
        cst = scratch(CONSTS)
        ids_g = scratch(GROUPS * F)
        ids_t = scratch(BT * F)
        pick_i = scratch(SLOTS)
        pick_f = scratch(SLOTS)
        idf = scratch(GROUPS * F)
        row4 = scratch(GROUPS * F)
        prod0 = scratch(GROUPS * F)
        prods = scratch((SLOTS - 1) * GROUPS * F)
        rows_f = scratch(SLOTS * GROUPS)
        hot = scratch(SLOTS * F)
        idtf = scratch(BT * F)
        in_pair = scratch(F)
        rest = scratch(F)
        is_not = scratch(F)
        wx = scratch(F)
        tmp8 = scratch(F)
        both = scratch(2 * PAIR_SLOTS * F)
        sel = scratch(2 * PAIR_SLOTS)
        buf_f = scratch(PAIR_SLOTS)
        buf_d = scratch(PAIR_SLOTS)
        wt_prod = scratch(2 * F)
        wt = scratch(2)
        same = scratch(1)
        cnt = scratch(1)
        dense_sb = Vf[0:DENSE, 0:B]
        w_dense_sb = Vf[0:DENSE, B:B + D1]
        h2 = [Vf[:, 2 * B + B * k:3 * B + B * k] for k in range(D2 // P)]
        y_sb = Vf[0:1, 4 * B:5 * B]

        ids_in, consts_in, cols_in, dense_in, out_done = (
            sem(n) for n in ("ids_in", "consts_in", "cols_in", "dense_in", "out_done"))
        chain = sem("chain")
        rows0_ready, rows_ready, rest_rows_ready, tab_ready, setup_done = (
            sem(n) for n in ("rows0_ready", "rows_ready", "rest_rows_ready", "tab_ready", "setup_done"))
        raw_in = [sem(f"raw_in{r}") for r in range(2)]
        w_hi, w_lo = sem("w_hi"), sem("w_lo")
        piece_done = sem("piece_done")
        gather_in = [sem(f"gather_in{r}") for r in range(STAGE)]
        x_turned, x_hi, x_lo = sem("x_turned"), sem("x_hi"), sem("x_lo")
        relu_ready, sum_ready = sem("relu_ready"), sem("sum_ready")
        full_out = sem("full_out")
        ev_hi, ev_lo = sem("ev_hi"), sem("ev_lo")
        rest_in = [sem(f"rest_in{b}") for b in range(BT)]
        rest_used = sem("rest_used")
        top2_done, h2_ready, y_done, y_ready = (sem(n) for n in ("top2_done", "h2_ready", "y_done", "y_ready"))

        def tile_pairs(eng, u):
            if u == 0:
                yield from range(KT // 2)
            else:
                with eng.Fori(0, KT // 2) as i:
                    yield i

        block = ctx.enter_context(nc.Block())

        @block.sync
        def _(sp):
            sp.dma_start(pick_i.bitcast(INT32), picks.partition_broadcast(P)).then_inc(ids_in, 16)
            for q in range(Q):
                sp.dma_start(ids_g[32 * q:32 * q + 32, :].bitcast(INT32), ids_by_group).then_inc(ids_in, 16)

            def load_piece(block_index, slot):
                return sp.dma_start(w_raw[:, slot, :],
                                    weights[bass.ds(block_index, 1), :, :].rearrange("o p c -> p (o c)"))\
                    .then_inc(raw_in[slot], 16)

            load_piece(0, 0)
            load_piece(1, 1)
            for u in range(UNITS):
                with sp.Fori(1 if u == 0 else 0, KT // 2) as i:
                    for r in range(2):
                        sp.wait_ge(w_lo, i * 2 + (KT * u + r - 1))
                        load_piece(i * 2 + (KT * UNIT_WEIGHTS[u] + r), r)
            for n in range(TOP1_PIECES + 1):
                sp.wait_ge(w_lo, UNITS * KT + n - 1)
                load_piece(8 * KT + n, n % 2)
                if n == 1:
                    sp.wait_ge(rest_used, 1)
                    sp.dma_start(dense_sb, dense_t).then_inc(dense_in, 16)
                    sp.dma_start(w_dense_sb, w_dense).then_inc(dense_in, 16)
            sp.wait_ge(y_ready, 1)
            sp.dma_start(out.rearrange("b o -> o b"), y_sb).then_inc(out_done, 16)
            sp.wait_ge(out_done, 16)

        @block.gpsimd
        def _(pool):
            for s in range(SLOTS):
                if s == 0:
                    pool.wait_ge(rows0_ready, 1)
                if s == 1:
                    pool.wait_ge(rows_ready, 1)
                for g in range(GROUPS):
                    c = s * GROUPS + g
                    if c >= STAGE:
                        pool.wait_ge(x_turned, c - STAGE + 1)
                    pool.indirect_dma_start(
                        gathered[:, c % STAGE, :], None, table_quarters,
                        bass.IndirectOffsetOnAxis(ap=rows[:, s, g:g + 1], axis=0),
                    ).then_inc(gather_in[c % STAGE], 16)
            pool.wait_ge(rest_rows_ready, 1)
            pool.wait_ge(ev_lo, AND1_EV)
            for f in range(F):
                for b in range(BT):
                    if f:
                        pool.wait_ge(rest_in[b], 16 * f)
                    pool.indirect_dma_start(
                        Vf[:, H * b:H * (b + 1)], None, table,
                        bass.IndirectOffsetOnAxis(ap=rows_rest[:, b, f:f + 1], axis=0),
                        compute_op=ALU.add if f else ALU.bypass,
                    ).then_inc(rest_in[b], 16)

        @block.scalar
        def _(act):
            act.dma_start(cst, consts).then_inc(consts_in, 16)
            act.dma_start(ids_t.bitcast(INT32), ids_by_tile).then_inc(consts_in, 16)
            act.dma_start(col[:, :], cols).then_inc(cols_in, 16)

            def split_hi(piece, slot, raw_count, done):
                act.wait_ge(raw_in[slot], raw_count)
                if not (isinstance(done, int) and done == 0):
                    act.wait_ge(piece_done, done)
                nc.scalar.activation(W_f[:, slot, 0, :], w_raw[:, slot, :], ACT.Copy).then_inc(w_hi, 1)

            def fill_hi(s, g, e):
                act.wait_ge(x_turned, g + (s * GROUPS + 1))
                nc.scalar.activation(X[:, SLOT_BUF[s], 0, :, bass.ds(g * 32, 32)], turned[:, e, :, :],
                                     ACT.Copy).then_inc(x_hi, 1)

            def evacuate(bank, piece_count, func, bias, scale, buf, tile, full_count):
                act.wait_ge(piece_done, piece_count)
                psum = PS[:, bass.ds(bank, 1), :].rearrange("p o b -> p (o b)")
                hi = X[:, buf, 0, bass.ds(tile, 1), :].rearrange("p o b -> p (o b)")
                nc.scalar.activation(psum, psum, func, bias=bias, scale=scale).then_inc(full_out, 1)
                act.wait_ge(full_out, full_count)
                nc.scalar.activation(hi, psum, ACT.Copy).then_inc(ev_hi, 1)

            split_hi(0, 0, 16, 0)
            with act.Fori(0, GROUPS // 2) as i:
                for e in range(2):
                    fill_hi(0, i * 2 + e, e)
            act.wait_ge(cols_in, 16)
            act.wait_ge(setup_done, 1)
            for u in range(UNITS):
                fill = UNIT_FILLS[u]
                if fill is not None and FILL_NEEDS[fill]:
                    act.wait_ge(piece_done, KT * FILL_NEEDS[fill])
                for i in tile_pairs(act, u):
                    for r in range(2):
                        m = i * 2 + r
                        piece = i * 2 + (KT * u + r)
                        nxt = (r + 1) % 2
                        split_hi(piece + 1, nxt, i * 16 + 16 * (KT * u // 2 + 1 + r), piece)
                        if fill is not None:
                            for e in range(2):
                                fill_hi(fill, i * 4 + (2 * r + e), e)
                        if u in (0, 1):
                            evacuate(m, piece + 1, ACT.Relu, col[:, bass.ds(m + BN1, 1)], 1.0, H_BUF + u, m, m + (KT * u + 1))
                        elif u in (2, 3):
                            evacuate(m, piece + 1, ACT.Tanh, col[:, bass.ds(m + BN2, 1)], 1.0, T0_BUF + u - 2, m,
                                     m + (KT * u + 1))
                        elif u == 7:
                            psum = PS[:, bass.ds(m, 1), :].rearrange("p o b -> p (o b)")
                            act.wait_ge(piece_done, piece + 1)
                            nc.scalar.activation(psum, psum, ACT.Relu, bias=col[:, bass.ds(m + BA1, 1)])\
                                .then_inc(relu_ready, 1)
                            act.wait_ge(sum_ready, m + 1)
                            nc.scalar.activation(X[:, AND_BUF, 0, bass.ds(m, 1), :].rearrange("p o b -> p (o b)"),
                                                 V[:, bass.ds(m, 1), :].rearrange("p o b -> p (o b)"),
                                                 ACT.Copy).then_inc(ev_hi, 1)
                        elif u == 9:
                            evacuate(m, piece + 1, ACT.Relu, col[:, bass.ds(m + BO1, 1)], 1.0, OR_BUF, m, m + (4 * KT + 1))
                        elif u == 11:
                            evacuate(m, piece + 1, ACT.Identity, final_bias[:, bass.ds(m, 1)], inv[:, 0:1],
                                     Z_BUF, m, m + (5 * KT + 1))
            base = UNITS * KT
            for n in range(TOP1_PIECES):
                split_hi(base + n + 1, (n + 1) % 2, 16 * ((base + n + 1) // 2 + 1), base + n)
                evacuate(n, base + n + 1, ACT.Relu, col[:, BT1 + n:BT1 + n + 1], 1.0, TOP_BUF, n,
                         6 * KT + n + 1)
            for n in range(D2 // P):
                act.wait_ge(top2_done, n + 1)
                nc.scalar.activation(h2[n], PS[:, 4 + n, :], ACT.Relu, bias=col[:, BT2 + n:BT2 + n + 1])\
                    .then_inc(h2_ready, 1)
            act.wait_ge(y_done, 1)
            nc.scalar.activation(y_sb, PS[0:1, 6, :], ACT.Copy).then_inc(y_ready, 1)

        @block.vector
        def _(dve):
            links = [0]

            def link(ins):
                links[0] += 1
                ins.then_inc(chain, 1)
                dve.wait_ge(chain, links[0])

            V_ = nc.vector
            gf = "p (g f) -> p g f"
            sf = "p (s f) -> p s f"
            field_of = cst[:, C_FIELD:C_FIELD + F]
            dve.wait_ge(ids_in, 16 * (1 + Q))
            dve.wait_ge(consts_in, 32)
            V_.tensor_copy(pick_f, pick_i.bitcast(INT32))
            link(V_.tensor_copy(idf, ids_g.bitcast(INT32)))
            V_.tensor_tensor(hot.rearrange(sf, f=F), pick_f.unsqueeze(2).broadcast_to([P, SLOTS, F]),
                             field_of.unsqueeze(1).broadcast_to([P, SLOTS, F]), ALU.is_equal)
            link(V_.scalar_tensor_tensor(out=row4.rearrange(gf, f=F), in0=idf.rearrange(gf, f=F), scalar=float(Q),
                                         in1=cst[:, C_ROW4:C_ROW4 + F].unsqueeze(1).broadcast_to([P, GROUPS, F]),
                                         op0=ALU.mult, op1=ALU.add))
            link(V_.tensor_tensor(prod0.rearrange(gf, f=F), row4.rearrange(gf, f=F),
                                  hot[:, 0:F].unsqueeze(1).broadcast_to([P, GROUPS, F]), ALU.mult))
            link(V_.tensor_reduce(rows_f[:, 0:GROUPS], prod0.rearrange(gf, f=F), AX.X, ALU.add))
            V_.tensor_copy(rows[:, 0, :], rows_f[:, 0:GROUPS]).then_inc(rows0_ready, 1)
            hot1 = hot.rearrange(sf, f=F)
            for s in range(1, SLOTS):
                part = prods[:, (s - 1) * GROUPS * F:s * GROUPS * F].rearrange(gf, f=F)
                last = V_.tensor_tensor(part, row4.rearrange(gf, f=F),
                                        hot1[:, s, :].unsqueeze(1).broadcast_to([P, GROUPS, F]), ALU.mult)
            link(last)
            link(V_.tensor_reduce(rows_f[:, GROUPS:], prods.rearrange("p (n f) -> p n f", f=F), AX.X, ALU.add))
            V_.tensor_copy(rows[:, 1:SLOTS, :].rearrange("p s g -> p (s g)"), rows_f[:, GROUPS:])\
                .then_inc(rows_ready, 1)

            def weights_and_buffers():
                V_.tensor_copy(idtf, ids_t.bitcast(INT32))
                V_.tensor_copy(ident[:, :], cst[:, C_IDENT:C_IDENT + P])
                V_.tensor_reduce(in_pair, hot[:, 2 * F:].rearrange("p (s f) -> p f s", f=F), AX.X, ALU.max)
                link(V_.tensor_tensor(is_not, hot[:, 0:F], hot[:, F:2 * F], ALU.max))
                link(V_.tensor_scalar(rest, in_pair, -1.0, 1.0, ALU.mult, ALU.add))
                V_.tensor_reduce(cnt, rest, AX.X, ALU.add)
                link(V_.tensor_tensor(tmp8, rest, is_not, ALU.mult))
                link(V_.tensor_tensor(wx, rest, tmp8, ALU.subtract))
                link(V_.tensor_scalar(cnt, cnt, 1.0, float(PAIR_SLOTS // 2), ALU.mult, ALU.add))
                link(V_.reciprocal(inv[:, :], cnt))
                bf = "p (b f) -> p b f"
                r3 = idtf.rearrange(bf, f=F)
                link(V_.tensor_tensor(r3, r3, cst[:, C_ROW:C_ROW + F].unsqueeze(1).broadcast_to([P, BT, F]), ALU.add))
                link(V_.scalar_tensor_tensor(out=r3, in0=r3, scalar=-float(zero_row),
                                             in1=wx.unsqueeze(1).broadcast_to([P, BT, F]),
                                             op0=ALU.add, op1=ALU.mult))
                V_.tensor_scalar(rows_rest[:, :, :], r3, 1.0, float(zero_row), ALU.mult, ALU.add)\
                    .then_inc(rest_rows_ready, 1)
                for j in range(2):
                    last = V_.tensor_tensor(
                        both[:, j * PAIR_SLOTS * F:(j + 1) * PAIR_SLOTS * F].rearrange(sf, f=F),
                        hot1[:, 2:, :], hot1[:, j, :].unsqueeze(1).broadcast_to([P, PAIR_SLOTS, F]), ALU.mult)
                    last = V_.tensor_tensor(wt_prod[:, j * F:(j + 1) * F], hot1[:, j, :], rest, ALU.mult)
                link(V_.tensor_tensor(tmp8, hot1[:, 0, :], hot1[:, 1, :], ALU.mult))
                V_.tensor_reduce(sel, both.rearrange("p (n f) -> p n f", f=F), AX.X, ALU.add)
                V_.tensor_reduce(wt, wt_prod.rearrange("p (n f) -> p n f", f=F), AX.X, ALU.add)
                link(V_.tensor_reduce(same, tmp8, AX.X, ALU.add))
                link(V_.tensor_scalar(same, same, -1.0, 1.0, ALU.mult, ALU.add))
                link(V_.tensor_tensor(wt[:, 0:1], wt[:, 0:1], same, ALU.mult))
                link(V_.tensor_copy(buf_f, cst[:, C_BUF:C_BUF + PAIR_SLOTS]))
                for j, t_buf in enumerate((T0_BUF, T1_BUF)):
                    link(V_.tensor_scalar(buf_d, buf_f, -1.0, float(t_buf), ALU.mult, ALU.add))
                    link(V_.tensor_tensor(buf_d, buf_d, sel[:, j * PAIR_SLOTS:(j + 1) * PAIR_SLOTS], ALU.mult))
                    link(V_.tensor_tensor(buf_f, buf_f, buf_d, ALU.add))
                V_.tensor_copy(tab[:, 0:PAIR_SLOTS], buf_f)
                V_.tensor_copy(tab[:, PAIR_SLOTS:PAIR_SLOTS + 2], wt).then_inc(tab_ready, 1)
                dve.wait_ge(cols_in, 16)
                link(V_.scalar_tensor_tensor(out=final_bias[:, :], in0=col[:, BA2:BA2 + KT], scalar=2.0,
                                             in1=col[:, BO2:BO2 + KT], op0=ALU.mult, op1=ALU.add))
                V_.tensor_scalar(final_bias[:, :], final_bias[:, :], inv[:, 0:1], None, ALU.mult)\
                    .then_inc(setup_done, 1)

            def turn(s, g, stage, count, e):
                dve.wait_ge(gather_in[stage], count)
                V_.transpose(turned_f[:, e, :], gathered[:, stage, :]).then_inc(x_turned, 1)

            def fill_lo(s, g, e):
                dve.wait_ge(x_hi, g + (s * GROUPS + 1))
                sl = bass.ds(g * 32, 32)
                V_.tensor_tensor(X[:, SLOT_BUF[s], 1, :, sl], turned[:, e, :, :],
                                 X[:, SLOT_BUF[s], 0, :, sl].bitcast(FP32), ALU.subtract).then_inc(x_lo, 1)

            def split_lo(slot, count):
                dve.wait_ge(w_hi, count)
                V_.tensor_tensor(W_f[:, slot, 1, :], w_raw[:, slot, :], W_f[:, slot, 0, :].bitcast(FP32),
                                 ALU.subtract).then_inc(w_lo, 1)

            def evacuate_lo(bank, hi_count, buf, tile):
                dve.wait_ge(ev_hi, hi_count)
                V_.tensor_tensor(X[:, buf, 1, bass.ds(tile, 1), :].rearrange("p o b -> p (o b)"),
                                 PS[:, bass.ds(bank, 1), :].rearrange("p o b -> p (o b)"),
                                 X[:, buf, 0, bass.ds(tile, 1), :].rearrange("p o b -> p (o b)").bitcast(FP32),
                                 ALU.subtract).then_inc(ev_lo, 1)

            split_lo(0, 1)
            for i in range(GROUPS // STAGE):
                for r in range(2):
                    if i or r:
                        dve.wait_ge(x_lo, i * 4 + 2 * r)
                    for e in range(2):
                        turn(0, i * 4 + (2 * r + e), 2 * r + e, i * 16 + 16, e)
                    for e in range(2):
                        fill_lo(0, i * 4 + (2 * r + e), e)
            weights_and_buffers()
            out_buf = {0: H_BUF, 1: H_BUF + 1, 2: T0_BUF, 3: T1_BUF, 9: OR_BUF, 11: Z_BUF}
            hi_before = {0: 0, 1: KT, 2: 2 * KT, 3: 3 * KT, 7: 4 * KT, 9: 5 * KT, 11: 6 * KT}
            for u in range(UNITS):
                fill = UNIT_FILLS[u]
                for i in tile_pairs(dve, u):
                    for r in range(2):
                        m = i * 2 + r
                        piece = i * 2 + (KT * u + r)
                        if fill is not None:
                            dve.wait_ge(x_lo, i * 4 + (fill * GROUPS + 2 * r))
                            for e in range(2):
                                turn(fill, None, 2 * r + e, i * 16 + (fill * GROUPS // STAGE + 1) * 16, e)
                        split_lo((r + 1) % 2, piece + 2)
                        if fill is not None:
                            for e in range(2):
                                fill_lo(fill, i * 4 + (2 * r + e), e)
                        psum = PS[:, bass.ds(m, 1), :].rearrange("p o b -> p (o b)")
                        v_m = V[:, bass.ds(m, 1), :].rearrange("p o b -> p (o b)")
                        if u == 5:
                            dve.wait_ge(piece_done, piece + 1)
                            V_.tensor_scalar(v_m, psum, col[:, bass.ds(m + BA1, 1)], 0.0, ALU.add, ALU.max)\
                                .then_inc(ev_lo, 1)
                        elif u == 7:
                            dve.wait_ge(relu_ready, m + 1)
                            V_.tensor_tensor(v_m, psum, v_m, ALU.add).then_inc(sum_ready, 1)
                            hi = X[:, AND_BUF, 0, bass.ds(m, 1), :].rearrange("p o b -> p (o b)")
                            dve.wait_ge(ev_hi, m + (hi_before[u] + 1))
                            V_.tensor_tensor(X[:, AND_BUF, 1, bass.ds(m, 1), :].rearrange("p o b -> p (o b)"),
                                             v_m, hi.bitcast(FP32), ALU.subtract).then_inc(ev_lo, 1)
                        elif u in out_buf:
                            evacuate_lo(m, m + (hi_before[u] + 1), out_buf[u], m)
            base = UNITS * KT
            for n in range(TOP1_PIECES):
                split_lo((n + 1) % 2, base + n + 2)
                evacuate_lo(n, 7 * KT + n + 1, TOP_BUF, n)

        @block.tensor
        def _(pe):
            def product(bank, slot, x, k_tiles, start, stop, w_of=lambda s, k: (s, k)):
                for k in range(k_tiles):
                    for n, (ws, xs) in enumerate(((0, 0), (0, 1), (1, 0))):
                        last = nc.tensor.matmul(PS[:, bank, :], w_of(slot, ws, k), x(xs, k),
                                                start=start and k == 0 and n == 0,
                                                stop=stop and k == k_tiles - 1 and n == 2)
                return last

            def w_piece(slot, ws, k):
                return W[:, slot, ws, k, :]

            def unit(first_piece, x, start, stop, bank_free):
                for m in range(KT):
                    pe.wait_ge(w_lo, first_piece + (m + 1))
                    if bank_free is not None and start:
                        pe.wait_ge(ev_lo, bank_free + (m + 1))
                    product(m, m % 2, x, KT, start, stop, w_piece).then_inc(piece_done, 1)

            for j in range(2):
                pe.wait_ge(x_lo, GROUPS * (j + 1))
                unit(KT * j, lambda xs, k: X[:, SLOT_BUF[j], xs, k, :], True, True, 0 if j else None)
            with pe.Fori(0, 2) as j:
                pe.wait_ge(ev_lo, j * KT + KT)
                unit(j * KT + 2 * KT, lambda xs, k: X[:, bass.ds(j + H_BUF, 1), xs, k, :].rearrange("p o b -> p (o b)"),
                     True, True, j * KT + KT)

            pe.wait_ge(tab_ready, 1)
            pe.wait_ge(ev_lo, NOT_EV)
            with pe.Fori(0, 3) as g:
                for half in range(2):
                    pe.wait_ge(x_lo, g * (2 * GROUPS) + GROUPS * (3 + half))
                    buf = pe.value_load(tab[0:1, bass.ds(g * 2 + half, 1)], min_val=0, max_val=BUFS - 1)
                    unit(g * (2 * KT) + (4 + half) * KT,
                         lambda xs, k, b=buf: X[:, bass.ds(b, 1), xs, k, :].rearrange("p o b -> p (o b)"),
                         half == 0, half == 1, g * KT + 3 * KT)

            pe.wait_ge(ev_lo, AND1_EV)
            unit(10 * KT, lambda xs, k: X[:, AND_BUF, xs, k, :], True, False, OR_EV - KT)
            for b in range(BT):
                pe.wait_ge(rest_in[b], 16 * F)
            for m in range(KT):
                for b in range(BT):
                    last = nc.tensor.matmul(PS[:, m, P * b:P * (b + 1)], Vf[:, H * b + P * m:H * b + P * (m + 1)],
                                            ident[:, :].bitcast(FP32), start=False, stop=False)
            last.then_inc(rest_used, 1)
            for j, t_buf in enumerate((T0_BUF, T1_BUF)):
                weight = pe.value_load(tab[0:1, PAIR_SLOTS + j:PAIR_SLOTS + j + 1], min_val=0, max_val=1)
                with pe.If(weight > 0):
                    for m in range(KT):
                        for xs in range(2):
                            nc.tensor.matmul(PS[:, m, :], ident[:, :], X[:, t_buf, xs, m, :], start=False, stop=False)
            pe.wait_ge(ev_lo, OR_EV)
            unit(11 * KT, lambda xs, k: X[:, OR_BUF, xs, k, :], False, True, None)

            pe.wait_ge(dense_in, 32)
            for m in range(TOP1_PIECES):
                pe.wait_ge(ev_lo, OR_EV + m + 1)
                nc.tensor.matmul(PS[:, m, :], w_dense_sb[:, P * m:P * (m + 1)], dense_sb, start=True, stop=False)
            pe.wait_ge(ev_lo, FINAL_EV)
            for m in range(TOP1_PIECES):
                pe.wait_ge(w_lo, UNITS * KT + m + 1)
                product(m, m % 2, lambda xs, k: X[:, Z_BUF, xs, k, :], KT, False, True, w_piece)\
                    .then_inc(piece_done, 1)
            pe.wait_ge(w_lo, PIECES)
            pe.wait_ge(ev_lo, FINAL_EV + TOP1_PIECES)
            w2 = W_f[:, 0, :, :].rearrange("p s (k m c) -> p s k m c", k=D1 // P, m=D2 // P)
            for m in range(D2 // P):
                product(4 + m, 0, lambda xs, k: X[:, TOP_BUF, xs, k, :], D1 // P, True, True,
                        lambda slot, ws, k, m=m: w2[:, ws, k, m, :]).then_inc(top2_done, 1)
            for k in range(D2 // P):
                pe.wait_ge(h2_ready, k + 1)
                last = nc.tensor.matmul(PS[0:1, 6, :], col[:, W3 + k:W3 + k + 1], h2[k],
                                        start=k == 0, stop=k == D2 // P - 1)
            last.then_inc(y_done, 1)


def kernel(**inputs):
    import numpy as np
    import concourse.bacc as bacc
    from concourse.bass_utils import run_bass_kernel_spmd

    a = {k: np.asarray(v) for k, v in inputs.items()}
    tables = [a[f"tbl_{f}"] for f in range(F)]
    starts = np.cumsum([0] + [t.shape[0] for t in tables])
    zero_row = int(starts[-1])

    def rows_plain(w):
        return w.reshape(KT, P, -1).transpose(1, 0, 2)

    def rows_field(w):
        return w.reshape(Q, KT, 32, -1).transpose(0, 2, 1, 3).reshape(P, KT, -1)

    def cut(w):
        return w.reshape(P, KT, -1, P).transpose(2, 0, 1, 3).reshape(-1, P, KT * P)

    def cut_field(w):
        return w.reshape(P, KT, Q, KT, 32).transpose(3, 0, 1, 2, 4).reshape(KT, P, KT * P)

    wa1, wo1 = a["L0_rec_Wa1"], a["L0_rec_Wo1"]
    blocks = [
        cut(rows_field(a["L0_rec_Wn1"])), cut_field(rows_plain(a["L0_rec_Wn2"])),
        cut(rows_field(wa1[:H])), cut(rows_field(wa1[H:])), cut(rows_field(wo1[:H])), cut(rows_field(wo1[H:])),
        cut(rows_plain(a["L0_rec_Wa2"])), cut(rows_plain(a["L0_rec_Wo2"])), cut(rows_plain(a["W_top1"][:H])),
        a["W_top2"].reshape(D1 // P, P, D2).transpose(1, 0, 2).reshape(1, P, -1),
    ]

    def column(v):
        return v.reshape(-1, P).T

    bn2 = a["L0_rec_bn2"].reshape(Q, KT, 32).transpose(0, 2, 1).reshape(P, KT)
    cols = [column(a["L0_rec_bn1"]), bn2, column(a["L0_rec_ba1"]), column(a["L0_rec_bo1"]),
            column(a["L0_rec_ba2"]), column(a["L0_rec_bo2"]), column(a["b_top1"]), column(a["b_top2"]),
            column(a["W_top3"])]

    consts = np.zeros((P, CONSTS), np.float32)
    consts[:, C_ROW4:C_ROW4 + F] = Q * starts[None, :F] + np.arange(P)[:, None] // 32
    consts[:, C_ROW:C_ROW + F] = starts[None, :F]
    consts[:, C_FIELD:C_FIELD + F] = np.arange(F)
    consts[:, C_BUF:C_BUF + PAIR_SLOTS] = SLOT_BUF[2:]
    consts[:, C_IDENT:] = np.eye(P)

    ids = a["ids"]
    arrays = {
        "table": np.concatenate([*tables, np.zeros((1, H), np.float32)]),
        "ids_by_group": ids.reshape(GROUPS, 32, F).transpose(1, 0, 2).reshape(32, GROUPS * F),
        "ids_by_tile": ids.reshape(BT, P, F).transpose(1, 0, 2).reshape(P, BT * F),
        "picks": np.concatenate([a["L0_rec_not_idx"].reshape(-1), a["L0_rec_and_pairs"].reshape(-1),
                                 a["L0_rec_or_pairs"].reshape(-1)]),
        "weights": np.concatenate(blocks),
        "cols": np.concatenate(cols, axis=1),
        "consts": consts,
        "dense_t": a["dense_ctx"].T,
        "w_dense": a["W_top1"][H:],
    }
    nc = bacc.Bacc("TRN2", target_bir_lowering=False, num_devices=1)
    args = []
    for name, x in arrays.items():
        arrays[name] = x = np.ascontiguousarray(x)
        args.append(nc.dram_tensor(name, x.shape, mybir.dt.from_np(x.dtype), kind="ExternalInput").ap())
    out = nc.dram_tensor("out", (B, 1), FP32, kind="ExternalOutput").ap()
    dlrm_tower(nc, *args, out, zero_row)
    result = run_bass_kernel_spmd(nc, [arrays], core_ids=[0])
    return result.results[0]["out"]
```

```python
from contextlib import ExitStack

import concourse.bass as bass
from concourse import mybir

FP32 = mybir.dt.float32
FP32R = mybir.dt.float32r
INT32 = mybir.dt.int32
ALU = mybir.AluOpType
ACT = mybir.ActivationFunctionType
AX = mybir.AxisListType

P = 128
B = 512
F = 8
H = 1024
KT = H // P
Q = 4
QC = H // Q
GROUPS = B // 32
BT = B // P
D1, D2, DENSE = 512, 256, 16

SLOTS = 8
PAIR_SLOTS = SLOTS - 2
STAGE = 4

BUFS = 5
SLOT_BUF = [0, 3, 4, 3, 2, 4, 2, 4]
H_BUF, T0_BUF, T1_BUF, AND_BUF, OR_BUF, Z_BUF, TOP_BUF = 1, 0, 1, 3, 2, 4, 0

UNIT_WEIGHTS = [0, 0, 1, 1, 2, 3, 2, 3, 4, 5, 6, 7]
UNITS = len(UNIT_WEIGHTS)
UNIT_FILLS = [1, 2, 3, None, 4, 5, None, 6, 7, None, None, None]
FILL_NEEDS = [0, 0, 0, 2, 4, 5, 7, 8]
TOP1_PIECES = D1 // P
PIECES = UNITS * KT + TOP1_PIECES + 1

NOT_EV, AND0_EV, AND1_EV, OR_EV, FINAL_EV = 4 * KT, 5 * KT, 6 * KT, 7 * KT, 8 * KT

BN1, BN2, BA1, BO1, BA2, BO2, BT1, BT2, W3 = 0, 8, 16, 24, 32, 40, 48, 52, 54
COLS = 56
C_ROW4, C_ROW, C_FIELD, C_BUF = 0, 8, 16, 24
CONSTS = 32


I_TILE, I_PICK, I_GROUP = 0, BT * F, BT * F + SLOTS
INTS = I_GROUP + GROUPS * F


def dlrm_tower(nc, table, ints, weights, cols, consts, identity, dense_t, w_dense, out, zero_row):
    table_quarters = table.rearrange("v (q c) -> (v q) c", q=Q)

    with ExitStack() as ctx:
        def sb(name, shape, dt):
            return ctx.enter_context(nc.sbuf_tensor(name, shape, dt))

        def sem(name):
            return ctx.enter_context(nc.semaphore(name))

        X = sb("X", [P, BUFS, 2, KT, B], FP32R)
        V = sb("V", [P, KT, B], FP32)
        w_raw = sb("w_raw", [P, 2, KT * P], FP32)
        W = sb("W", [P, 2, 2, KT, P], FP32R)
        gathered = sb("gathered", [P, STAGE, QC], FP32)
        turned = sb("turned", [P, 2, KT, 32], FP32)
        ident = sb("ident", [P, P], FP32R)
        col = sb("col", [P, COLS], FP32)
        rows0 = sb("rows0", [P, BT], INT32)
        rows = sb("rows", [P, SLOTS - 1, GROUPS], INT32)
        rows_rest = sb("rows_rest", [P, BT, F], INT32)
        tab = sb("tab", [P, 8], INT32)
        inv = sb("inv", [P, 1], FP32)
        final_bias = sb("final_bias", [P, KT], FP32)
        PS = ctx.enter_context(nc.psum_tensor("PS", [P, KT, B], FP32))

        Vf = V[:, :, :].rearrange("p k b -> p (k b)")
        W_f = W[:, :, :, :, :].rearrange("p r s k m -> p r s (k m)")
        scratch_f = gathered[:, :, :].rearrange("p s c -> p (s c)")
        at = [0]

        def scratch(n):
            at[0] += n
            return scratch_f[:, at[0] - n:at[0]]
        int_in = scratch(INTS).bitcast(INT32)
        cst = scratch(CONSTS)
        ident_in = scratch(P)
        row4 = scratch(GROUPS * F)
        row_t = scratch(BT * F)
        prod_t = scratch(BT * F)
        rows_f = scratch((SLOTS - 1) * GROUPS)
        rows0_f = scratch(BT)
        hot = scratch(SLOTS * F)
        in_pair, rest, is_not, wx, tmp8 = (scratch(F) for _ in range(5))
        both = scratch(2 * PAIR_SLOTS * F)
        sel = scratch(2 * PAIR_SLOTS)
        buf_f = scratch(PAIR_SLOTS)
        buf_d = scratch(PAIR_SLOTS)
        wt_prod = scratch(2 * F)
        wt = scratch(2)
        same = scratch(1)
        cnt = scratch(1)
        prods = turned[:, :, :, :].rearrange("p e k b -> p (e k b)")
        dense_sb = Vf[0:DENSE, 0:B]
        w_dense_sb = Vf[0:DENSE, B:B + D1]
        h2 = [Vf[:, 2 * B + B * k:3 * B + B * k] for k in range(D2 // P)]
        y_sb = Vf[0:1, 4 * B:5 * B]

        ints_in, consts_in, ident_in_done, cols_in, dense_in, out_done = (
            sem(n) for n in ("ints_in", "consts_in", "ident_in", "cols_in", "dense_in", "out_done"))
        chain = sem("chain")
        rows0_ready, ident_ready, setup_done = (sem(n) for n in ("rows0_ready", "ident_ready", "setup_done"))
        x0_in = [sem(f"x0_in{b}") for b in range(BT)]
        x0_turned, x0_hi, x0_lo = sem("x0_turned"), sem("x0_hi"), sem("x0_lo")
        raw_in = [sem(f"raw_in{r}") for r in range(2)]
        w_hi, w_lo = sem("w_hi"), sem("w_lo")
        piece_done = sem("piece_done")
        gather_in = [sem(f"gather_in{r}") for r in range(STAGE)]
        x_turned, x_hi, x_lo = sem("x_turned"), sem("x_hi"), sem("x_lo")
        relu_ready, sum_ready = sem("relu_ready"), sem("sum_ready")
        full_out = sem("full_out")
        ev_hi, ev_lo = sem("ev_hi"), sem("ev_lo")
        rest_in = [sem(f"rest_in{b}") for b in range(BT)]
        rest_used = sem("rest_used")
        top2_done, h2_ready, y_done, y_ready = (sem(n) for n in ("top2_done", "h2_ready", "y_done", "y_ready"))

        def tile_pairs(eng, u):
            if u in (0, 7):
                yield from range(KT // 2)
            else:
                with eng.Fori(0, KT // 2) as i:
                    yield i

        block = ctx.enter_context(nc.Block())

        @block.sync
        def _(sp):
            sp.dma_start(int_in, ints).then_inc(ints_in, 16)

            def load_piece(block_index, slot):
                return sp.dma_start(w_raw[:, slot, :],
                                    weights[bass.ds(block_index, 1), :, :].rearrange("o p c -> p (o c)"))\
                    .then_inc(raw_in[slot], 16)

            load_piece(0, 0)
            load_piece(1, 1)
            for u in range(UNITS):
                with sp.Fori(1 if u == 0 else 0, KT // 2) as i:
                    for r in range(2):
                        sp.wait_ge(w_lo, i * 2 + (KT * u + r - 1))
                        load_piece(i * 2 + (KT * UNIT_WEIGHTS[u] + r), r)
            for n in range(TOP1_PIECES + 1):
                sp.wait_ge(w_lo, UNITS * KT + n - 1)
                load_piece(8 * KT + n, n % 2)
                if n == 1:
                    sp.wait_ge(rest_used, 1)
                    sp.dma_start(dense_sb, dense_t).then_inc(dense_in, 16)
                    sp.dma_start(w_dense_sb, w_dense).then_inc(dense_in, 16)
            sp.wait_ge(y_ready, 1)
            sp.dma_start(out.rearrange("b o -> o b"), y_sb).then_inc(out_done, 16)
            sp.wait_ge(out_done, 16)

        @block.gpsimd
        def _(pool):
            pool.wait_ge(rows0_ready, 1)
            for b in range(BT):
                pool.indirect_dma_start(Vf[:, H * b:H * (b + 1)], None, table,
                                        bass.IndirectOffsetOnAxis(ap=rows0[:, b:b + 1], axis=0)).then_inc(x0_in[b], 16)
            pool.wait_ge(setup_done, 1)
            for c in range((SLOTS - 1) * GROUPS):
                if c >= STAGE:
                    pool.wait_ge(x_turned, c - STAGE + 1)
                pool.indirect_dma_start(
                    gathered[:, c % STAGE, :], None, table_quarters,
                    bass.IndirectOffsetOnAxis(ap=rows[:, c // GROUPS, c % GROUPS:c % GROUPS + 1], axis=0),
                ).then_inc(gather_in[c % STAGE], 16)
            pool.wait_ge(ev_lo, AND1_EV)
            for f in range(F):
                for b in range(BT):
                    if f:
                        pool.wait_ge(rest_in[b], 16 * f)
                    pool.indirect_dma_start(
                        Vf[:, H * b:H * (b + 1)], None, table,
                        bass.IndirectOffsetOnAxis(ap=rows_rest[:, b, f:f + 1], axis=0),
                        compute_op=ALU.add if f else ALU.bypass,
                    ).then_inc(rest_in[b], 16)

        @block.scalar
        def _(act):
            act.dma_start(cst, consts).then_inc(consts_in, 16)
            act.dma_start(ident_in, identity).then_inc(ident_in_done, 16)
            act.dma_start(col[:, :], cols).then_inc(cols_in, 16)

            def split_hi(piece, slot, raw_count, done):
                act.wait_ge(raw_in[slot], raw_count)
                if done is not None:
                    act.wait_ge(piece_done, done)
                nc.scalar.activation(W_f[:, slot, 0, :], w_raw[:, slot, :], ACT.Copy).then_inc(w_hi, 1)

            def fill_hi(s, g, e):
                act.wait_ge(x_turned, g + ((s - 1) * GROUPS + 1))
                nc.scalar.activation(X[:, SLOT_BUF[s], 0, :, bass.ds(g * 32, 32)], turned[:, e, :, :],
                                     ACT.Copy).then_inc(x_hi, 1)

            def evacuate(bank, piece_count, func, bias, scale, buf, tile, full_count):
                act.wait_ge(piece_done, piece_count)
                psum = PS[:, bass.ds(bank, 1), :].rearrange("p o b -> p (o b)")
                hi = X[:, buf, 0, bass.ds(tile, 1), :].rearrange("p o b -> p (o b)")
                nc.scalar.activation(psum, psum, func, bias=bias, scale=scale).then_inc(full_out, 1)
                act.wait_ge(full_out, full_count)
                nc.scalar.activation(hi, psum, ACT.Copy).then_inc(ev_hi, 1)

            def pair_sum_hi(m):
                act.wait_ge(sum_ready, m + 1)
                nc.scalar.activation(X[:, AND_BUF, 0, m, :], V[:, m, :], ACT.Copy).then_inc(ev_hi, 1)

            split_hi(0, 0, 16, None)
            split_hi(1, 1, 16, None)
            for k in range(KT):
                act.wait_ge(x0_turned, k + 1)
                nc.scalar.activation(X[:, SLOT_BUF[0], 0, k, :], PS[:, k, :], ACT.Copy).then_inc(x0_hi, 1)
            act.wait_ge(cols_in, 16)
            act.wait_ge(setup_done, 1)
            for u in range(UNITS):
                fill = UNIT_FILLS[u]
                if fill is not None and FILL_NEEDS[fill]:
                    act.wait_ge(piece_done, KT * FILL_NEEDS[fill])
                for i in tile_pairs(act, u):
                    for r in range(2):
                        m = i * 2 + r
                        piece = i * 2 + (KT * u + r)
                        if u or i or r:
                            split_hi(piece + 1, (r + 1) % 2, i * 16 + 16 * (KT * u // 2 + 1 + r), piece)
                        if fill is not None:
                            for e in range(2):
                                fill_hi(fill, i * 4 + (2 * r + e), e)
                        if u in (0, 1):
                            evacuate(m, piece + 1, ACT.Relu, col[:, bass.ds(m + BN1, 1)], 1.0, H_BUF + u, m, m + (KT * u + 1))
                        elif u in (2, 3):
                            evacuate(m, piece + 1, ACT.Tanh, col[:, bass.ds(m + BN2, 1)], 1.0, T0_BUF + u - 2, m,
                                     m + (KT * u + 1))
                        elif u == 7:
                            if m:
                                pair_sum_hi(m - 1)
                        elif u == 9:
                            evacuate(m, piece + 1, ACT.Relu, col[:, bass.ds(m + BO1, 1)], 1.0, OR_BUF, m, m + (4 * KT + 1))
                        elif u == 11:
                            evacuate(m, piece + 1, ACT.Identity, final_bias[:, bass.ds(m, 1)], inv[:, 0:1],
                                     Z_BUF, m, m + (5 * KT + 1))
                if u == 7:
                    pair_sum_hi(KT - 1)
            base = UNITS * KT
            for n in range(TOP1_PIECES):
                split_hi(base + n + 1, (n + 1) % 2, 16 * ((base + n + 1) // 2 + 1), base + n)
                evacuate(n, base + n + 1, ACT.Relu, col[:, BT1 + n:BT1 + n + 1], 1.0, TOP_BUF, n,
                         6 * KT + n + 1)
            for n in range(D2 // P):
                act.wait_ge(top2_done, n + 1)
                nc.scalar.activation(h2[n], PS[:, 4 + n, :], ACT.Relu, bias=col[:, BT2 + n:BT2 + n + 1])\
                    .then_inc(h2_ready, 1)
            act.wait_ge(y_done, 1)
            nc.scalar.activation(y_sb, PS[0:1, 6, :], ACT.Copy).then_inc(y_ready, 1)

        @block.vector
        def _(dve):
            links = [0]

            def link(ins):
                links[0] += 1
                ins.then_inc(chain, 1)
                dve.wait_ge(chain, links[0])

            V_ = nc.vector
            gf = "p (g f) -> p g f"
            sf = "p (s f) -> p s f"
            hot_sf = hot.rearrange(sf, f=F)
            row4_gf = row4.rearrange(gf, f=F)
            row_bf = row_t.rearrange(gf, f=F)
            dve.wait_ge(ints_in, 16)
            dve.wait_ge(consts_in, 16)
            V_.tensor_tensor(hot_sf, int_in[:, I_PICK:I_PICK + SLOTS].unsqueeze(2).broadcast_to([P, SLOTS, F]),
                             cst[:, C_FIELD:C_FIELD + F].unsqueeze(1).broadcast_to([P, SLOTS, F]), ALU.is_equal)
            link(V_.tensor_tensor(row_bf, int_in[:, I_TILE:I_TILE + BT * F].rearrange(gf, f=F),
                                  cst[:, C_ROW:C_ROW + F].unsqueeze(1).broadcast_to([P, BT, F]), ALU.add))
            link(V_.tensor_tensor(prod_t.rearrange(gf, f=F), row_bf,
                                  hot[:, 0:F].unsqueeze(1).broadcast_to([P, BT, F]), ALU.mult))
            link(V_.tensor_reduce(rows0_f, prod_t.rearrange(gf, f=F), AX.X, ALU.add))
            V_.tensor_copy(rows0[:, :], rows0_f).then_inc(rows0_ready, 1)
            dve.wait_ge(ident_in_done, 16)
            V_.tensor_copy(ident[:, :], ident_in).then_inc(ident_ready, 1)
            V_.scalar_tensor_tensor(out=row4_gf, in0=int_in[:, I_GROUP:I_GROUP + GROUPS * F].rearrange(gf, f=F),
                                    scalar=float(Q), in1=cst[:, C_ROW4:C_ROW4 + F].unsqueeze(1)
                                    .broadcast_to([P, GROUPS, F]), op0=ALU.mult, op1=ALU.add)
            V_.tensor_reduce(in_pair, hot[:, 2 * F:].rearrange("p (s f) -> p f s", f=F), AX.X, ALU.max)
            link(V_.tensor_tensor(is_not, hot[:, 0:F], hot[:, F:2 * F], ALU.max))
            V_.tensor_scalar(wx, is_not, -1.0, 1.0, ALU.mult, ALU.add)
            link(V_.tensor_scalar(rest, in_pair, -1.0, 1.0, ALU.mult, ALU.add))

            def slot_rows(first, n):
                for s in range(first, first + n):
                    last = V_.tensor_tensor(prods[:, (s - first) * GROUPS * F:(s - first + 1) * GROUPS * F]
                                            .rearrange(gf, f=F), row4_gf,
                                            hot_sf[:, s, :].unsqueeze(1).broadcast_to([P, GROUPS, F]), ALU.mult)
                link(last)
                link(V_.tensor_reduce(rows_f[:, (first - 1) * GROUPS:(first - 1 + n) * GROUPS],
                                      prods[:, 0:n * GROUPS * F].rearrange("p (n f) -> p n f", f=F), AX.X, ALU.add))

            slot_rows(1, 3)
            slot_rows(4, 4)
            V_.tensor_copy(rows[:, :, :].rearrange("p s g -> p (s g)"), rows_f)
            V_.tensor_reduce(cnt, rest, AX.X, ALU.add)
            link(V_.tensor_tensor(wx, wx, rest, ALU.mult))
            V_.scalar_tensor_tensor(out=prod_t.rearrange(gf, f=F), in0=row_bf, scalar=-float(zero_row),
                                    in1=wx.unsqueeze(1).broadcast_to([P, BT, F]), op0=ALU.add, op1=ALU.mult)
            link(V_.tensor_scalar(cnt, cnt, 1.0, float(PAIR_SLOTS // 2), ALU.mult, ALU.add))
            V_.tensor_scalar(rows_rest[:, :, :], prod_t.rearrange(gf, f=F), 1.0, float(zero_row), ALU.mult, ALU.add)
            V_.reciprocal(inv[:, :], cnt)
            for j in range(2):
                V_.tensor_tensor(both[:, j * PAIR_SLOTS * F:(j + 1) * PAIR_SLOTS * F].rearrange(sf, f=F),
                                 hot_sf[:, 2:, :], hot_sf[:, j, :].unsqueeze(1).broadcast_to([P, PAIR_SLOTS, F]),
                                 ALU.mult)
                V_.tensor_tensor(wt_prod[:, j * F:(j + 1) * F], hot_sf[:, j, :], rest, ALU.mult)
            V_.tensor_copy(buf_f, cst[:, C_BUF:C_BUF + PAIR_SLOTS])
            link(V_.tensor_tensor(tmp8, hot_sf[:, 0, :], hot_sf[:, 1, :], ALU.mult))
            V_.tensor_reduce(sel, both.rearrange("p (n f) -> p n f", f=F), AX.X, ALU.add)
            V_.tensor_reduce(wt, wt_prod.rearrange("p (n f) -> p n f", f=F), AX.X, ALU.add)
            link(V_.tensor_reduce(same, tmp8, AX.X, ALU.add))
            for j, t_buf in enumerate((T0_BUF, T1_BUF)):
                link(V_.tensor_scalar(buf_d, buf_f, -1.0, float(t_buf), ALU.mult, ALU.add))
                link(V_.tensor_tensor(buf_d, buf_d, sel[:, j * PAIR_SLOTS:(j + 1) * PAIR_SLOTS], ALU.mult))
                if j == 0:
                    V_.tensor_scalar(same, same, -1.0, 1.0, ALU.mult, ALU.add)
                else:
                    V_.tensor_tensor(wt[:, 0:1], wt[:, 0:1], same, ALU.mult)
                link(V_.tensor_tensor(buf_f, buf_f, buf_d, ALU.add))
            V_.tensor_copy(tab[:, 0:PAIR_SLOTS], buf_f)
            V_.tensor_copy(tab[:, PAIR_SLOTS:PAIR_SLOTS + 2], wt)
            dve.wait_ge(cols_in, 16)
            link(V_.scalar_tensor_tensor(out=final_bias[:, :], in0=col[:, BA2:BA2 + KT], scalar=2.0,
                                         in1=col[:, BO2:BO2 + KT], op0=ALU.mult, op1=ALU.add))
            V_.tensor_scalar(final_bias[:, :], final_bias[:, :], inv[:, 0:1], None, ALU.mult).then_inc(setup_done, 1)

            def turn(stage, count, e):
                dve.wait_ge(gather_in[stage], count)
                V_.transpose(turned[:, e, :, :], gathered[:, stage, :].rearrange("p (h k) -> p k h", k=KT))\
                    .then_inc(x_turned, 1)

            def fill_lo(s, g, e):
                dve.wait_ge(x_hi, g + ((s - 1) * GROUPS + 1))
                sl = bass.ds(g * 32, 32)
                V_.tensor_tensor(X[:, SLOT_BUF[s], 1, :, sl], turned[:, e, :, :],
                                 X[:, SLOT_BUF[s], 0, :, sl].bitcast(FP32), ALU.subtract).then_inc(x_lo, 1)

            def split_lo(slot, count):
                dve.wait_ge(w_hi, count)
                V_.tensor_tensor(W_f[:, slot, 1, :], w_raw[:, slot, :], W_f[:, slot, 0, :].bitcast(FP32),
                                 ALU.subtract).then_inc(w_lo, 1)

            def evacuate_lo(bank, hi_count, buf, tile):
                dve.wait_ge(ev_hi, hi_count)
                V_.tensor_tensor(X[:, buf, 1, bass.ds(tile, 1), :].rearrange("p o b -> p (o b)"),
                                 PS[:, bass.ds(bank, 1), :].rearrange("p o b -> p (o b)"),
                                 X[:, buf, 0, bass.ds(tile, 1), :].rearrange("p o b -> p (o b)").bitcast(FP32),
                                 ALU.subtract).then_inc(ev_lo, 1)

            def pair_sum_lo(m):
                dve.wait_ge(ev_hi, 4 * KT + m + 1)
                V_.tensor_tensor(X[:, AND_BUF, 1, m, :], V[:, m, :], X[:, AND_BUF, 0, m, :].bitcast(FP32),
                                 ALU.subtract).then_inc(ev_lo, 1)

            split_lo(0, 1)
            split_lo(1, 2)
            for k in range(KT):
                dve.wait_ge(x0_hi, k + 1)
                V_.tensor_tensor(X[:, SLOT_BUF[0], 1, k, :], PS[:, k, :], X[:, SLOT_BUF[0], 0, k, :].bitcast(FP32),
                                 ALU.subtract).then_inc(x0_lo, 1)
            out_buf = {0: H_BUF, 1: H_BUF + 1, 2: T0_BUF, 3: T1_BUF, 9: OR_BUF, 11: Z_BUF}
            hi_before = {0: 0, 1: KT, 2: 2 * KT, 3: 3 * KT, 9: 5 * KT, 11: 6 * KT}
            for u in range(UNITS):
                fill = UNIT_FILLS[u]
                for i in tile_pairs(dve, u):
                    for r in range(2):
                        m = i * 2 + r
                        piece = i * 2 + (KT * u + r)
                        if fill is not None:
                            if u or i or r:
                                dve.wait_ge(x_lo, i * 4 + ((fill - 1) * GROUPS + 2 * r))
                            for e in range(2):
                                turn(2 * r + e, i * 16 + ((fill - 1) * GROUPS // STAGE + 1) * 16, e)
                        if u or i or r:
                            split_lo((r + 1) % 2, piece + 2)
                        if fill is not None:
                            for e in range(2):
                                fill_lo(fill, i * 4 + (2 * r + e), e)
                        psum = PS[:, bass.ds(m, 1), :].rearrange("p o b -> p (o b)")
                        v_m = V[:, bass.ds(m, 1), :].rearrange("p o b -> p (o b)")
                        if u == 5:
                            dve.wait_ge(piece_done, piece + 1)
                            V_.tensor_scalar(v_m, psum, col[:, bass.ds(m + BA1, 1)], 0.0, ALU.add, ALU.max)\
                                .then_inc(ev_lo, 1)
                        elif u == 7:
                            if m:
                                pair_sum_lo(m - 1)
                            dve.wait_ge(piece_done, piece + 1)
                            V_.tensor_scalar(psum, psum, col[:, BA1 + m:BA1 + m + 1], 0.0, ALU.add, ALU.max)\
                                .then_inc(relu_ready, 1)
                            dve.wait_ge(relu_ready, m + 1)
                            V_.tensor_tensor(v_m, psum, v_m, ALU.add).then_inc(sum_ready, 1)
                        elif u in out_buf:
                            evacuate_lo(m, m + (hi_before[u] + 1), out_buf[u], m)
                if u == 7:
                    pair_sum_lo(KT - 1)
            base = UNITS * KT
            for n in range(TOP1_PIECES):
                split_lo((n + 1) % 2, base + n + 2)
                evacuate_lo(n, 7 * KT + n + 1, TOP_BUF, n)

        @block.tensor
        def _(pe):
            def product(bank, slot, x, k_tiles, start, stop, w_of, before_k=None):
                for k in range(k_tiles):
                    if before_k is not None:
                        before_k(k)
                    for n, (ws, xs) in enumerate(((0, 0), (0, 1), (1, 0))):
                        last = nc.tensor.matmul(PS[:, bank, :], w_of(slot, ws, k), x(xs, k),
                                                start=start and k == 0 and n == 0,
                                                stop=stop and k == k_tiles - 1 and n == 2)
                return last

            def w_piece(slot, ws, k):
                return W[:, slot, ws, k, :]

            def unit(first_piece, x, start, stop, bank_free, before_k=None):
                for m in range(KT):
                    pe.wait_ge(w_lo, first_piece + (m + 1))
                    if bank_free is not None and start:
                        pe.wait_ge(ev_lo, bank_free + (m + 1))
                    product(m, m % 2, x, KT, start, stop, w_piece, before_k if m == 0 else None)\
                        .then_inc(piece_done, 1)

            pe.wait_ge(ident_ready, 1)
            for b in range(BT):
                pe.wait_ge(x0_in[b], 16)
                tile = Vf[:, H * b:H * (b + 1)].rearrange("p (c k) -> p k c", k=KT)
                for k in range(KT):
                    turn = nc.tensor.transpose(PS[:, k, P * b:P * (b + 1)], tile[:, k, :],
                                               ident[:, :].bitcast(FP32))
                    if b == BT - 1:
                        turn.then_inc(x0_turned, 1)

            unit(0, lambda xs, k: X[:, SLOT_BUF[0], xs, k, :], True, True, None,
                 lambda k: pe.wait_ge(x0_lo, k + 1))
            pe.wait_ge(x_lo, GROUPS)
            unit(KT, lambda xs, k: X[:, SLOT_BUF[1], xs, k, :], True, True, 0)
            with pe.Fori(0, 2) as j:
                pe.wait_ge(ev_lo, j * KT + KT)
                unit(j * KT + 2 * KT, lambda xs, k: X[:, bass.ds(j + H_BUF, 1), xs, k, :].rearrange("p o b -> p (o b)"),
                     True, True, j * KT + KT)

            pe.wait_ge(setup_done, 1)
            pe.wait_ge(ev_lo, NOT_EV - 1)

            def t1_complete(k):
                if k == KT - 1:
                    pe.wait_ge(ev_lo, NOT_EV)

            with pe.Fori(0, 3) as g:
                for half in range(2):
                    pe.wait_ge(x_lo, g * (2 * GROUPS) + GROUPS * (2 + half))
                    buf = pe.value_load(tab[0:1, bass.ds(g * 2 + half, 1)], min_val=0, max_val=BUFS - 1)
                    unit(g * (2 * KT) + (4 + half) * KT,
                         lambda xs, k, b=buf: X[:, bass.ds(b, 1), xs, k, :].rearrange("p o b -> p (o b)"),
                         half == 0, half == 1, g * KT + 3 * KT, t1_complete if half == 0 else None)

            pe.wait_ge(ev_lo, AND1_EV)
            unit(10 * KT, lambda xs, k: X[:, AND_BUF, xs, k, :], True, False, OR_EV - KT)
            for b in range(BT):
                pe.wait_ge(rest_in[b], 16 * F)
            for m in range(KT):
                for b in range(BT):
                    tile = Vf[:, H * b:H * (b + 1)].rearrange("p (c k) -> p k c", k=KT)
                    last = nc.tensor.matmul(PS[:, m, P * b:P * (b + 1)], tile[:, m, :],
                                            ident[:, :].bitcast(FP32), start=False, stop=False)
            last.then_inc(rest_used, 1)
            for j, t_buf in enumerate((T0_BUF, T1_BUF)):
                weight = pe.value_load(tab[0:1, PAIR_SLOTS + j:PAIR_SLOTS + j + 1], min_val=0, max_val=1)
                with pe.If(weight > 0):
                    for m in range(KT):
                        for xs in range(2):
                            nc.tensor.matmul(PS[:, m, :], ident[:, :], X[:, t_buf, xs, m, :], start=False, stop=False)
            pe.wait_ge(ev_lo, OR_EV)
            unit(11 * KT, lambda xs, k: X[:, OR_BUF, xs, k, :], False, True, None)

            pe.wait_ge(dense_in, 32)
            for m in range(TOP1_PIECES):
                pe.wait_ge(ev_lo, OR_EV + m + 1)
                nc.tensor.matmul(PS[:, m, :], w_dense_sb[:, P * m:P * (m + 1)], dense_sb, start=True, stop=False)
            pe.wait_ge(ev_lo, FINAL_EV)
            for m in range(TOP1_PIECES):
                pe.wait_ge(w_lo, UNITS * KT + m + 1)
                product(m, m % 2, lambda xs, k: X[:, Z_BUF, xs, k, :], KT, False, True, w_piece)\
                    .then_inc(piece_done, 1)
            pe.wait_ge(w_lo, PIECES)
            w2 = W_f[:, 0, :, :].rearrange("p s (k m c) -> p s k m c", k=D1 // P, m=D2 // P)
            for k in range(D1 // P):
                pe.wait_ge(ev_lo, FINAL_EV + k + 1)
                for m in range(D2 // P):
                    for n, (ws, xs) in enumerate(((0, 0), (0, 1), (1, 0))):
                        last = nc.tensor.matmul(PS[:, 4 + m, :], w2[:, ws, k, m, :], X[:, TOP_BUF, xs, k, :],
                                                start=k == 0 and n == 0, stop=k == D1 // P - 1 and n == 2)
                    if k == D1 // P - 1:
                        last.then_inc(top2_done, 1)
            for k in range(D2 // P):
                pe.wait_ge(h2_ready, k + 1)
                last = nc.tensor.matmul(PS[0:1, 6, :], col[:, W3 + k:W3 + k + 1], h2[k],
                                        start=k == 0, stop=k == D2 // P - 1)
            last.then_inc(y_done, 1)


def kernel(**inputs):
    import numpy as np
    import concourse.bacc as bacc
    from concourse.bass_utils import run_bass_kernel_spmd

    a = {k: np.asarray(v) for k, v in inputs.items()}
    tables = [a[f"tbl_{f}"] for f in range(F)]
    starts = np.cumsum([0] + [t.shape[0] for t in tables])
    zero_row = int(starts[-1])

    def cut(w, m_tiles=KT):
        return w.reshape(P, KT, P, m_tiles).transpose(3, 0, 1, 2).reshape(m_tiles, P, KT * P)

    wa1, wo1 = a["L0_rec_Wa1"], a["L0_rec_Wo1"]
    blocks = [cut(w) for w in (a["L0_rec_Wn1"], a["L0_rec_Wn2"], wa1[:H], wa1[H:], wo1[:H], wo1[H:],
                               a["L0_rec_Wa2"], a["L0_rec_Wo2"])]
    blocks += [cut(a["W_top1"][:H], TOP1_PIECES),
               a["W_top2"].reshape(P, D1 // P, P, D2 // P).transpose(0, 1, 3, 2).reshape(1, P, -1)]
    cols = [v.reshape(P, -1) for v in (a["L0_rec_bn1"], a["L0_rec_bn2"], a["L0_rec_ba1"], a["L0_rec_bo1"],
                                       a["L0_rec_ba2"], a["L0_rec_bo2"], a["b_top1"], a["b_top2"], a["W_top3"])]

    consts = np.zeros((P, CONSTS), np.float32)
    consts[:, C_ROW4:C_ROW4 + F] = Q * starts[None, :F] + np.arange(P)[:, None] // 32
    consts[:, C_ROW:C_ROW + F] = starts[None, :F]
    consts[:, C_FIELD:C_FIELD + F] = np.arange(F)
    consts[:, C_BUF:C_BUF + PAIR_SLOTS] = SLOT_BUF[2:]

    ids = a["ids"]
    by_group = ids.reshape(GROUPS, 32, F).transpose(1, 0, 2).reshape(32, GROUPS * F)
    by_tile = ids.reshape(BT, P, F).transpose(1, 0, 2).reshape(P, BT * F)
    picks = np.concatenate([a[f"L0_rec_{n}"].reshape(-1) for n in ("not_idx", "and_pairs", "or_pairs")])
    arrays = {
        "table": np.concatenate([*tables, np.zeros((1, H), np.float32)]),
        "ints": np.concatenate([by_tile, np.broadcast_to(picks, (P, SLOTS)), np.tile(by_group, (Q, 1))], axis=1),
        "weights": np.concatenate(blocks),
        "cols": np.concatenate(cols, axis=1),
        "consts": consts,
        "identity": np.eye(P, dtype=np.float32),
        "dense_t": a["dense_ctx"].T,
        "w_dense": a["W_top1"][H:].reshape(DENSE, P, TOP1_PIECES).transpose(0, 2, 1).reshape(DENSE, D1),
    }
    nc = bacc.Bacc("TRN2", target_bir_lowering=False, num_devices=1)
    args = []
    for name, x in arrays.items():
        arrays[name] = x = np.ascontiguousarray(x)
        args.append(nc.dram_tensor(name, x.shape, mybir.dt.from_np(x.dtype), kind="ExternalInput").ap())
    out = nc.dram_tensor("out", (B, 1), FP32, kind="ExternalOutput").ap()
    dlrm_tower(nc, *args, out, zero_row)
    result = run_bass_kernel_spmd(nc, [arrays], core_ids=[0])
    return result.results[0]["out"]
```
